# Optimizing a Trainium2 kernel written in Bass

```python
import numpy as np
import jax
import jax.numpy as jnp

def _softmax(x, axis=-1):
    return jax.nn.softmax(x, axis=axis)

def _gelu(x):
    return jax.nn.gelu(x, approximate=True)

def _silu(x):
    return jax.nn.silu(x)

def _sigmoid(x):
    return jax.nn.sigmoid(x)

def _layernorm(x, axis=-1, eps=1e-05):
    m = jnp.mean(x, axis=axis, keepdims=True)
    v = jnp.var(x, axis=axis, keepdims=True)
    return (x - m) / jnp.sqrt(v + eps)

def _scatter_add(tgt, idx, src, axis=0):
    return tgt.at[idx].add(src)

def _segment_sum(src, seg, n):
    return jax.ops.segment_sum(src, seg, n)
kernel_name = 'mk_flamingo_gated_d1_seqx_r4_6e7309'

def setup_inputs(seed: int=0):
    np.random.seed(seed)
    _w = jnp.asarray

    def _rec_inputs():
        import jax
        import jax.numpy as jnp
        _rk = jax.random.key(seed)
        x = -0.0005207 + 1.001 * jax.random.normal(jax.random.fold_in(_rk, 1), (4, 512, 512), jnp.float32)
        _lenS = 512 - jax.random.randint(jax.random.fold_in(_rk, 7), (4,), 0, max(1, 512 // 4) + 1, jnp.int32)
        _lenS2 = 512 - jax.random.randint(jax.random.fold_in(_rk, 8), (4,), 0, max(1, 512 // 4) + 1, jnp.int32)
        _ctx_2048P = jax.random.normal(jax.random.fold_in(_rk, 12), (4, 16, 512), jnp.float32)
        _ctx_2048c = jax.random.dirichlet(jax.random.fold_in(_rk, 512), 0.3 * jnp.ones((16,), jnp.float32), (4, 512))
        _ctx_2048t = jnp.einsum('bsk,bkd->bsd', _ctx_2048c, _ctx_2048P)
        _ctx_2048t = _ctx_2048t * jax.lax.rsqrt(jnp.mean(jnp.square(_ctx_2048t)) + 1e-12) * 0.953939
        ctx_2048 = -5.72187e-05 + 0.999849 * (_ctx_2048t + 0.3 * jax.random.normal(jax.random.fold_in(_rk, 612), (4, 512, 512), jnp.float32))
        _validS = jnp.arange(512)[None, :] < _lenS[:, None]
        _validS2 = jnp.arange(512)[None, :] < _lenS2[:, None]
        _causal = jnp.tril(jnp.ones((512, 512), dtype=bool))
        mask_BxSx4224_bf0 = jnp.logical_not(jnp.ones((4, 512, 1056), dtype=bool))
        _g = jax.random.normal(jax.random.fold_in(_rk, 9001), (2, 1), jnp.float32)
        _g = jnp.sign(_g) * jnp.maximum(jnp.abs(_g), 1.0) + (_g == 0) * 1.0
        g_xattn = _g[0]
        g_ffn = _g[1]
        return (x, ctx_2048, mask_BxSx4224_bf0, g_xattn, g_ffn)
    x, ctx_2048, mask_BxSx4224_bf0, g_xattn, g_ffn = _rec_inputs()

    def _L0_xattn_setup():
        import jax, jax.numpy as jnp
        import numpy as np
        import math
        DIM = 512
        B, Q_LEN, KV_LEN = (8, 128, 1024)
        key = jax.random.key(seed)
        ks = jax.random.split(key, 8)
        x = jax.random.normal(ks[0], (B, Q_LEN, DIM), dtype=jnp.float32)
        mask = jnp.zeros((B, Q_LEN, KV_LEN + Q_LEN), dtype=bool)
        k_cache = jax.random.normal(ks[1], (B, KV_LEN, DIM), dtype=jnp.float32)
        v_cache = jax.random.normal(ks[2], (B, KV_LEN, DIM), dtype=jnp.float32)
        scale = 1.0 / math.sqrt(DIM)
        wq = jax.random.normal(ks[3], (DIM, DIM), dtype=jnp.float32) * scale
        wk = jax.random.normal(ks[4], (DIM, DIM), dtype=jnp.float32) * scale
        wv = jax.random.normal(ks[5], (DIM, DIM), dtype=jnp.float32) * scale
        wo = jax.random.normal(ks[6], (DIM, DIM), dtype=jnp.float32) * scale
        return {'x': x, 'mask': mask, 'k_cache': k_cache, 'v_cache': v_cache, 'wq': wq, 'wk': wk, 'wv': wv, 'wo': wo}
    _L0_xattn_all = _L0_xattn_setup()
    _L0_xattn_in = {k: v for k, v in _L0_xattn_all.items() if k in ('wq', 'wk', 'wv', 'wo')}
    del _L0_xattn_all

    def _L0_ffn_setup():
        import jax, jax.numpy as jnp
        import numpy as np

        @jax.custom_vjp
        def ste_sign(x):
            return jnp.sign(x)

        def _ste_fwd(x):
            return (jnp.sign(x), None)

        def _ste_bwd(_, g):
            return (g,)
        ste_sign.defvjp(_ste_fwd, _ste_bwd)
        D_MODEL = 512
        D_HIDDEN = 2048
        key = jax.random.key(seed)
        k_x, k_up, k_dn = jax.random.split(key, 3)
        x = jax.random.normal(k_x, (2, 512, D_MODEL), dtype=jnp.float32)
        up_weight = jax.random.normal(k_up, (D_HIDDEN, D_MODEL), dtype=jnp.float32) * 0.02
        down_weight = jax.random.normal(k_dn, (D_MODEL, D_HIDDEN), dtype=jnp.float32) * 0.02
        up_scale = jnp.ones((D_HIDDEN,), dtype=jnp.float32)
        down_scale = jnp.ones((D_MODEL,), dtype=jnp.float32)
        output_scale = jnp.ones((1,), dtype=jnp.float32)
        return {'x': x, 'up_weight': up_weight, 'down_weight': down_weight, 'up_scale': up_scale, 'down_scale': down_scale, 'output_scale': output_scale}
    _L0_ffn_all = _L0_ffn_setup()
    _L0_ffn_in = {k: v for k, v in _L0_ffn_all.items() if k in ('up_weight', 'down_weight', 'up_scale', 'down_scale', 'output_scale')}
    del _L0_ffn_all
    return {'x': x, 'ctx_2048': ctx_2048, 'mask_BxSx4224_bf0': mask_BxSx4224_bf0, 'g_xattn': g_xattn, 'g_ffn': g_ffn, 'L0_xattn_wq': _L0_xattn_in['wq'], 'L0_xattn_wk': _L0_xattn_in['wk'], 'L0_xattn_wv': _L0_xattn_in['wv'], 'L0_xattn_wo': _L0_xattn_in['wo'], 'L0_ffn_up_weight': _L0_ffn_in['up_weight'], 'L0_ffn_down_weight': _L0_ffn_in['down_weight'], 'L0_ffn_up_scale': _L0_ffn_in['up_scale'], 'L0_ffn_down_scale': _L0_ffn_in['down_scale'], 'L0_ffn_output_scale': _L0_ffn_in['output_scale']}

def reference(x, ctx_2048, mask_BxSx4224_bf0, g_xattn, g_ffn, L0_xattn_wq, L0_xattn_wk, L0_xattn_wv, L0_xattn_wo, L0_ffn_up_weight, L0_ffn_down_weight, L0_ffn_up_scale, L0_ffn_down_scale, L0_ffn_output_scale):
    import jax
    import jax.numpy as jnp

    def _L0_xattn_ref(x, mask, k_cache, v_cache, wq, wk, wv, wo):
        import jax, jax.numpy as jnp
        import numpy as np
        import math
        DIM = 512
        B, Q_LEN, KV_LEN = (8, 128, 1024)
        q = jnp.einsum('bsd,ed->bse', x, wq)
        k_new = jnp.einsum('bsd,ed->bse', x, wk)
        v_new = jnp.einsum('bsd,ed->bse', x, wv)
        k = jnp.concatenate([k_cache, k_new], axis=1)
        v = jnp.concatenate([v_cache, v_new], axis=1)
        scale = 1.0 / math.sqrt(q.shape[-1])
        scores = jnp.einsum('bqd,bkd->bqk', q, k) * scale
        attn = jax.nn.softmax(scores, axis=-1)
        out = jnp.einsum('bqk,bkd->bqd', attn, v)
        return jnp.einsum('bqd,ed->bqe', out, wo)

    def _L0_ffn_ref(x, up_weight, down_weight, up_scale, down_scale, output_scale):
        import jax, jax.numpy as jnp
        import numpy as np

        @jax.custom_vjp
        def ste_sign(x):
            return jnp.sign(x)

        def _ste_fwd(x):
            return (jnp.sign(x), None)

        def _ste_bwd(_, g):
            return (g,)
        ste_sign.defvjp(_ste_fwd, _ste_bwd)
        D_MODEL = 512
        D_HIDDEN = 2048
        up_w = ste_sign(up_weight)
        down_w = ste_sign(down_weight)
        hidden = jnp.einsum('bsd,hd->bsh', x, up_w) * up_scale
        hidden = jax.nn.relu(hidden)
        out = jnp.einsum('bsh,dh->bsd', hidden, down_w) * down_scale
        return out * output_scale
    x = x + jnp.tanh(g_xattn[0]) * _L0_xattn_ref(_layernorm(x, axis=-1), mask_BxSx4224_bf0, ctx_2048, ctx_2048, L0_xattn_wq, L0_xattn_wk, L0_xattn_wv, L0_xattn_wo)
    x = x + jnp.tanh(g_ffn[0]) * _L0_ffn_ref(_layernorm(x, axis=-1), L0_ffn_up_weight, L0_ffn_down_weight, L0_ffn_up_scale, L0_ffn_down_scale, L0_ffn_output_scale)
    return x

_drawn_inputs = setup_inputs


def setup_inputs(seed=0):
    import zlib

    import numpy as np

    out = dict(_drawn_inputs(seed))
    spreads = {'L0_ffn_up_scale': (1.0, 0.2), 'L0_ffn_down_scale': (1.0, 0.2)}
    factors = {}
    for name, (base, spread) in spreads.items():
        noise = np.random.default_rng([zlib.crc32(name.encode()), seed]).standard_normal(out[name].shape)
        drawn = base * np.exp(spread * noise) if base else spread * noise
        out[name] = jnp.asarray(drawn.astype(out[name].dtype))
    for name, factor in factors.items():
        out[name] = (out[name] * factor).astype(out[name].dtype)
    return out
```

```python
from contextlib import ExitStack

import concourse.bass as bass
from concourse import mybir

F32 = mybir.dt.float32
F32R = mybir.dt.float32r
ALU = mybir.AluOpType
ACT = mybir.ActivationFunctionType
AX = mybir.AxisListType

P = 128
HI, LO = 0, 1
PASSES = ((HI, HI), (HI, LO), (LO, HI))


def gated_block(nc, x, ctx_kv, g_xattn, g_ffn, wq, wk, wv, wo, up_w, down_w, up_scale, down_scale,
                output_scale, out):
    BATCH, ROWS, DIM = x.shape
    HIDDEN = up_w.shape[0]
    RT = ROWS // P
    DC = DIM // P
    KEYS = ctx_kv.shape[1] + ROWS
    KC = KEYS // P
    HC = HIDDEN // P
    EPS = 1e-5
    SCALE = float(DIM) ** -0.5
    assert RT == 4 and DC == 4 and KC == 8 and HC == 16 and BATCH == 4

    W_K, W_Q, W_V, W_O = range(4)
    TURNS_FIRST = 4 * RT + RT + RT
    TURNS_BATCH = 2 * RT + RT + RT
    TURNS_ALL = TURNS_FIRST + TURNS_BATCH * (BATCH - 1) + 3 * RT
    PROJS_FIRST = 2 * DC
    PROJS_BATCH = 4 * 4
    PROJS_ALL = PROJS_FIRST + PROJS_BATCH * (BATCH - 1) + 2 * 4
    T_WK, T_X0, T_WQ, T_C0, T_WV, T_WO = (RT * i for i in range(6))

    def turn0(b):
        return TURNS_FIRST + TURNS_BATCH * b

    def proj0(b):
        return PROJS_FIRST + PROJS_BATCH * b

    row_tiles = "(r p) d -> p r d"
    x_v = x.rearrange("b (r p) d -> b p r d", p=P)
    ctx_v = ctx_kv.rearrange("b (r p) d -> b p r d", p=P)
    out_v = out.rearrange("b (r p) d -> p (b r) d", p=P)
    up_v = up_w.rearrange("(j p) d -> j p d", p=P)
    down_v = down_w.rearrange("(r p) (j h) -> j p r h", p=P, h=P)

    with ExitStack() as stack:
        def sb(name, shape, dt=F32):
            return stack.enter_context(nc.sbuf_tensor(name, shape, dt))

        def pb(name, shape):
            return stack.enter_context(nc.psum_tensor(name, shape, F32))

        def sem(name):
            return stack.enter_context(nc.semaphore(name))

        rows = sb("rows", [P, BATCH * RT, DIM])
        weights = sb("weights", [P, 4, 2, DC, DIM], F32R)
        four_x = sb("four_x", [P, 4, 2, DC, ROWS], F32R)
        xT, qT = four_x[:, 0], four_x[:, 1]
        ctx_side = four_x[:, 2]
        new_side = four_x[:, 3]
        probsT = sb("probsT", [P, 2, KC, ROWS], F32R)
        probs = sb("probs", [P, 2, KEYS])
        raw_ctx = sb("raw_ctx", [P, RT, DIM])
        normed = sb("normed", [P, RT, DIM])
        spare = sb("spare", [P, 2, DIM])
        out_gain = sb("out_gain", [P, DIM])
        ident = sb("ident", [P, P])
        hid_gain = sb("hid_gain", [P, HC])
        stats = sb("stats", [P, RT, 6])
        mean_var = sb("mean_var", [P, RT, 2])
        var_eps = sb("var_eps", [P, RT])
        minus_half = sb("minus_half", [P, RT])
        eps = sb("eps", [P, RT])
        rstd = sb("rstd", [P, RT])
        neg_max = sb("neg_max", [P, RT])
        row_sum = sb("row_sum", [P, RT])
        row_inv = sb("row_inv", [P, RT])
        row_gain = sb("row_gain", [P, RT])
        gates_raw = sb("gates_raw", [P, 3])
        gates = sb("gates", [P, 2])
        ffn_gain = sb("ffn_gain", [P, 1])

        signs = weights[:, :, :, :, :].rearrange("p w s c n -> p (w s c n)").rearrange(
            "p (j k n) -> p j k n", j=HC, k=2)
        raw_signs = raw_ctx[:, :, :].rearrange("p (s k) n -> p s k n", s=2)
        hid = probs[:, :, :].rearrange("p s (k n) -> p (s k) n", n=ROWS)
        HR = 4
        hid_split = probsT[:, :, :, :].rearrange("p s k n -> p (s k) n").rearrange(
            "p (k s) n -> p k s n", s=2)

        score = [pb(f"score{i}", [P, 2, 512]) for i in range(2)]
        proj = pb("proj", [P, 2, 512])
        turn = pb("turn", [P, 2, 512])

        def wide(r):
            return score[r // 2][:, r % 2, :]

        def first_turn_bank(n):
            k = n % 6
            return turn[:, k, :] if k < 2 else wide(k - 2)

        x0_in, small_in, xrest_in, ctx_in, out_stored = map(sem, (
            "x0_in", "small_in", "xrest_in", "ctx_in", "out_stored"))
        w_in = [sem(f"w_in{i}") for i in range(4)]
        signs_in = [sem(f"signs_in{i}") for i in range(2)]
        ident_zero, ident_ready, half_ready = map(sem, ("ident_zero", "ident_ready", "half_ready"))
        tanh_done, gain_done = sem("tanh_done"), sem("gain_done")
        turned, turn_hi, turn_lo = map(sem, ("turned", "turn_hi", "turn_lo"))
        proj_done, proj_hi, proj_lo = map(sem, ("proj_done", "proj_hi", "proj_lo"))
        scored, max_done, exp_done = map(sem, ("scored", "max_done", "exp_done"))
        vals_hi, vals_ready = sem("vals_hi"), sem("vals_ready")
        stats_done, meanvar_done, eps_done, rstd_done, normed_done = map(sem, (
            "stats_done", "meanvar_done", "eps_done", "rstd_done", "normed_done"))
        inv_done, rowgain_done = sem("inv_done"), sem("rowgain_done")
        wo_done, attended = sem("wo_done"), sem("attended")
        signs_turned, signs_ready = sem("signs_turned"), sem("signs_ready")
        up_done, relu_done, hid_hi, hid_ready = map(sem, ("up_done", "relu_done", "hid_hi", "hid_ready"))
        down_done, acc_free, out_ready = map(sem, ("down_done", "acc_free", "out_ready"))

        block = stack.enter_context(nc.Block())

        @block.sync
        def _(sp):
            sp.dma_start(rows[:, RT * 1:RT * 2, :], wk.rearrange(row_tiles, p=P)).then_inc(w_in[W_K], 16)
            sp.dma_start(rows[:, 0:RT, :], x_v[0]).then_inc(x0_in, 16)
            sp.dma_start(rows[:, RT * 2:RT * 3, :], wq.rearrange(row_tiles, p=P)).then_inc(w_in[W_Q], 16)
            sp.dma_start(raw_ctx[:, :, :], ctx_v[0]).then_inc(ctx_in, 16)
            sp.dma_start(rows[:, RT * 3:RT * 4, :], wv.rearrange(row_tiles, p=P)).then_inc(w_in[W_V], 16)
            sp.dma_start(probs[:, :, :].rearrange("p s (k n) -> p (s k) n", n=DIM),
                         wo.rearrange(row_tiles, p=P)).then_inc(w_in[W_O], 16)
            for i, g in enumerate((g_xattn, g_ffn, output_scale)):
                sp.dma_start(gates_raw[:, i:i + 1], g.rearrange("(a n) -> a n", a=1).broadcast_to([P, 1])
                             ).then_inc(small_in, 16)
            sp.dma_start(out_gain[:, :], down_scale.rearrange("(a n) -> a n", a=1).broadcast_to([P, DIM])
                         ).then_inc(small_in, 16)
            with nc.allow_non_contiguous_dma("2048 scales, once"):
                sp.dma_start(hid_gain[:, :], up_scale.rearrange("(j p) -> p j", p=P)).then_inc(small_in, 16)
            for b, last_turn in ((1, T_WK), (2, T_WQ), (3, T_WV)):
                sp.wait_ge(turned, last_turn + RT)
                sp.dma_start(rows[:, RT * b:RT * (b + 1), :], x_v[b]).then_inc(xrest_in, 16)
            with sp.Fori(0, BATCH - 1) as b:
                sp.wait_ge(vals_ready, b + 1)
                sp.dma_start(raw_ctx[:, :, :], ctx_v[b + 1]).then_inc(ctx_in, 16)
            sp.wait_ge(vals_ready, BATCH)
            for j in range(HC):
                if j >= 2:
                    sp.wait_ge(signs_turned, 2 * (j - 1))
                sp.dma_start(raw_signs[:, j % 2, 0, :], up_v[j]).then_inc(signs_in[j % 2], 16)
                sp.dma_start(raw_signs[:, j % 2, 1, :].rearrange("p (r h) -> p r h", h=P), down_v[j]
                             ).then_inc(signs_in[j % 2], 16)
            with sp.Fori(0, BATCH * RT) as t:
                sp.wait_ge(out_ready, t + 1)
                sp.dma_start(out_v[:, t, :], rows[:, t, :]).then_inc(out_stored, 16)
            sp.wait_ge(out_stored, 16 * BATCH * RT)

        @block.gpsimd
        def _(pool):
            pool.memset(ident[:, :], 0.0).then_inc(ident_zero, 1)
            pool.memset(minus_half[:, :], -0.5).then_inc(half_ready, 1)
            pool.memset(eps[:, :], EPS).then_inc(half_ready, 1)
            pool.wait_ge(ident_zero, 1)
            pool.affine_select(out=ident[:, :], in_=ident[:, :], compare_op=ALU.not_equal, fill=1.0, base=0,
                               pattern=[[-1, P]], channel_multiplier=1).then_inc(ident_ready, 1)
            pool.wait_ge(half_ready, 2)

            def inverse_std(n):
                pool.wait_ge(meanvar_done, RT * n + RT)
                pool.tensor_tensor(var_eps[:, :], mean_var[:, :, 1], eps[:, :], ALU.add).then_inc(eps_done, 1)
                pool.wait_ge(eps_done, n + 1)
                pool.tensor_tensor(rstd[:, :], var_eps[:, :], minus_half[:, :], ALU.pow).then_inc(rstd_done, 1)

            def batch(b):
                inverse_std(b + 1)
                pool.wait_ge(vals_hi, b + 1)
                pool.tensor_tensor(ctx_side[:, LO], raw_ctx[:, :, :], ctx_side[:, HI].bitcast(F32),
                                   ALU.subtract).then_inc(vals_ready, 1)

            inverse_std(0)
            with pool.Fori(0, BATCH) as b:
                batch(b)
            for n in range(BATCH + 1, 2 * BATCH):
                inverse_std(n)

        @block.tensor
        def _(pe):
            def transposes(bank, tiles, done):
                for k, tile in enumerate(tiles):
                    last = pe.transpose(bank[:, k * P:(k + 1) * P], tile, ident[:, :])
                last.then_inc(done, 1)

            def turn_job(n, k, tiles):
                pe.wait_ge(turn_lo, n - 1)
                transposes(turn[:, k, :], tiles, turned)

            def cols(src):
                return [src[:, k * P:(k + 1) * P] for k in range(4)]

            def product(bank, lhs, rhs, start, stop):
                for i, (l, r) in enumerate(PASSES):
                    last = pe.matmul(bank, lhs(l), rhs(r), start=start and i == 0, stop=stop and i == 2)
                return last

            def proj_job(n, k, terms, wait=None):
                if wait is None:
                    wait = n - 1
                if wait is not False:
                    pe.wait_ge(proj_lo, wait)
                for i, (lhs, rhs) in enumerate(terms):
                    last = product(proj[:, k, :], lhs, rhs, i == 0, i == len(terms) - 1)
                last.then_inc(proj_done, 1)

            def out_of(buf, c, lo, hi):
                return lambda s: buf[:, s, c, lo:hi]

            def feature_major(w, e):
                return [(out_of(weights[:, w], c, e * P, (e + 1) * P), out_of(xT, c, 0, ROWS)) for c in range(DC)]

            def v_terms(r):
                return [(out_of(xT, c, r * P, (r + 1) * P), out_of(weights[:, W_V], c, 0, DIM)) for c in range(DC)]

            def attn_terms(e):
                new = [(out_of(new_side, r, e * P, (e + 1) * P), out_of(probsT, DC + r, 0, ROWS)) for r in range(RT)]
                old = [(out_of(ctx_side, r, e * P, (e + 1) * P), out_of(probsT, r, 0, ROWS)) for r in range(RT)]
                return new, old

            def scores(b, t):
                if t >= 2:
                    pe.wait_ge(exp_done, RT * b + t - 1)
                for half, side in enumerate((ctx_side, new_side)):
                    for c in range(DC):
                        if t == 0 and half == 0:
                            pe.wait_ge(proj_lo, proj0(b) - DC + c + 1)
                        last = product(score[t % 2][:, half, :], out_of(qT, c, t * P, (t + 1) * P),
                                       out_of(side, c, 0, ROWS), c == 0, c == DC - 1)
                last.then_inc(scored, 1)

            def turn_probs(b, t):
                pe.wait_ge(exp_done, RT * b + t + 1)
                for half in range(2):
                    turn_job(turn0(b) + 2 * t + half, half, cols(probs[:, t % 2, half * 512:(half + 1) * 512]))

            def turn_next_rows(b, r):
                pe.wait_ge(normed_done, RT * (b + 1) + r + 1)
                turn_job(turn0(b) + 2 * RT + r, r % 2, cols(normed[:, r, :]))

            def turn_next_context(b, r):
                if r == 0:
                    pe.wait_ge(ctx_in, 16 * (b + 2))
                turn_job(turn0(b) + 3 * RT + r, r % 2, cols(raw_ctx[:, r, :]))

            def turn_signs(j):
                pe.wait_ge(signs_in[j % 2], 32 * (j // 2 + 1))
                for k in range(2):
                    if j == 0:
                        pe.wait_ge(turn_lo, TURNS_ALL)
                    else:
                        pe.wait_ge(signs_ready, 2 * (j - 1) + k + 1)
                    transposes(turn[:, k, :], cols(raw_signs[:, j % 2, k, :]), signs_turned)

            def batch(b, last_batch):
                for t in range(RT):
                    scores(b, t)
                    if t >= 1:
                        turn_probs(b, t - 1)
                n = proj0(b)
                proj_job(n, 0, v_terms(0))
                proj_job(n + 1, 1, v_terms(1))
                turn_probs(b, RT - 1)
                proj_job(n + 2, 0, v_terms(2))
                proj_job(n + 3, 1, v_terms(3))
                pe.wait_ge(turn_lo, turn0(b) + 2 * RT)
                for e in range(DC):
                    new, old = attn_terms(e)
                    pe.wait_ge(proj_lo, n + 4 + e - 1)
                    for i, (lhs, rhs) in enumerate(new):
                        if e == 0:
                            pe.wait_ge(proj_lo, n + i + 1)
                        product(proj[:, e % 2, :], lhs, rhs, i == 0, False)
                    if e == 0:
                        pe.wait_ge(vals_ready, b + 1)
                    for i, (lhs, rhs) in enumerate(old):
                        last = product(proj[:, e % 2, :], lhs, rhs, False, i == RT - 1)
                    last.then_inc(proj_done, 1)
                    if e in (1, 2):
                        turn_next_rows(b, 2 * (e - 1))
                        turn_next_rows(b, 2 * (e - 1) + 1)
                for c in range(DC):
                    pe.wait_ge(proj_lo, n + 4 + c + 1)
                    for r in range(RT):
                        if c == 0 and r in (0, 2):
                            pe.wait_ge(exp_done, RT * b + RT)
                        last = product(wide(r), out_of(qT, c, r * P, (r + 1) * P),
                                       out_of(weights[:, W_O], c, 0, DIM), c == 0, c == DC - 1)
                        if c == DC - 1:
                            last.then_inc(wo_done, 1)
                    if c < 2 and not last_batch:
                        turn_next_context(b, 2 * c)
                        turn_next_context(b, 2 * c + 1)
                    if c < 2 and last_batch:
                        turn_signs(c)
                if not last_batch:
                    pe.wait_ge(turn_lo, turn0(b) + 3 * RT)
                    for e in range(DC):
                        proj_job(n + 8 + e, e % 2, feature_major(W_K, e))
                    for e in range(DC):
                        if e == DC - 1:
                            pe.wait_ge(attended, RT * (b + 1))
                            pe.wait_ge(turn_lo, turn0(b + 1))
                        proj_job(n + 12 + e, e % 2, feature_major(W_Q, e))

            def first_turn(n, tiles):
                if n >= 6:
                    pe.wait_ge(turn_lo, n - 5)
                transposes(first_turn_bank(n), tiles, turned)

            def first_weight(w, first, buf, r):
                if r == 0:
                    pe.wait_ge(w_in[w], 16)
                first_turn(first + r, cols(buf[:, r, :]))

            wo_raw = probs[:, :, :].rearrange("p s (k n) -> p (s k) n", n=DIM)
            pe.wait_ge(ident_ready, 1)
            for r in range(RT):
                first_weight(W_K, T_WK, rows[:, RT * 1:RT * 2, :], r)
            for r in range(RT):
                pe.wait_ge(normed_done, r + 1)
                first_turn(T_X0 + r, cols(normed[:, r, :]))
            for r in range(RT):
                first_weight(W_Q, T_WQ, rows[:, RT * 2:RT * 3, :], r)
            pe.wait_ge(turn_lo, T_X0 + RT)
            for m in range(2 * DC):
                if m == DC:
                    pe.wait_ge(turn_lo, T_WQ + RT)
                proj_job(m, m % 2, feature_major(W_K if m < DC else W_Q, m % DC), wait=m - 1 if m >= 2 else False)
                for r in (2 * (m % 2), 2 * (m % 2) + 1):
                    if m < 2:
                        if r == 0:
                            pe.wait_ge(ctx_in, 16)
                        first_turn(T_C0 + r, cols(raw_ctx[:, r, :]))
                    elif m < 4:
                        first_weight(W_V, T_WV, rows[:, RT * 3:RT * 4, :], r)
                    elif m < 6:
                        first_weight(W_O, T_WO, wo_raw, r)
            pe.wait_ge(turn_lo, TURNS_FIRST)

            with pe.Fori(0, BATCH - 1) as b:
                batch(b, False)
            batch(BATCH - 1, True)

            def up(c, j, src, first):
                g = HC * c + j
                if first:
                    pe.wait_ge(signs_ready, 2 * j + 1)
                if first and j < 2:
                    pe.wait_ge(proj_lo, PROJS_ALL)
                else:
                    pe.wait_ge(relu_done, g - 1)
                for k in range(DC):
                    for s in (HI, LO):
                        last = pe.matmul(proj[:, j % 2, :], signs[:, j, 0, k * P:(k + 1) * P], src(s, k),
                                         start=(k == 0 and s == HI), stop=(k == DC - 1 and s == LO))
                last.then_inc(up_done, 1)

            def down(c, j, first=False):
                g = HC * c + j
                pe.wait_ge(hid_ready, g + 1)
                for r in range(RT):
                    if j == 0 and first:
                        pe.wait_ge(attended, RT * (BATCH - 1) + r + 1)
                    elif j == 0:
                        pe.wait_ge(acc_free, RT * (c - 1) + r + 1)
                    for s in (HI, LO):
                        last = pe.matmul(wide(r), hid_split[:, j % HR, s, r * P:(r + 1) * P], signs[:, j, 1, :],
                                         start=(j == 0 and s == HI), stop=(j == HC - 1 and s == LO))
                    last.then_inc(down_done, 1)

            def turn_next_block(c, r, src):
                pe.wait_ge(normed_done, RT * (BATCH + c + 1) + r + 1)
                turn_job(TURNS_ALL + RT * c + r, r % 2, cols(src[:, r, :]))

            def ffn_block(c, cur, first, last_block):
                pe.wait_ge(turn_lo, TURNS_ALL + RT * c)
                for j in range(HC):
                    if first and j + 2 < HC:
                        turn_signs(j + 2)
                    up(c, j, lambda s, k: four_x[:, cur, s, k, :], first)
                    if first and j >= 2:
                        down(c, j - 2, True)
                    if not first:
                        down(c - 1, HC - 2 + j) if j < 2 else down(c, j - 2)
                    if first and j >= HC - 2:
                        if j == HC - 2:
                            pe.wait_ge(signs_ready, 2 * HC)
                        turn_next_block(c, 2 * (j - HC + 2), normed)
                        turn_next_block(c, 2 * (j - HC + 2) + 1, normed)
                    if not first and not last_block and 8 <= j < 12:
                        turn_next_block(c, j - 8, normed)

            ffn_block(0, 0, True, False)
            with pe.Fori(1, BATCH - 1) as c:
                ffn_block(c, c, False, False)
            ffn_block(BATCH - 1, BATCH - 1, False, True)
            down(BATCH - 1, HC - 2)
            down(BATCH - 1, HC - 1)

        @block.scalar
        def _(act):
            act.wait_ge(small_in, 16 * 5)
            act.activation(gates[:, :], gates_raw[:, 0:2], ACT.Tanh).then_inc(tanh_done, 1)

            def four(bank):
                return bank.rearrange("p (k n) -> p k n", n=P)

            def turn_out(n, bank, dst):
                act.wait_ge(turned, n + 1)
                act.activation(dst, four(bank), ACT.Copy).then_inc(turn_hi, 1)

            def proj_out(n, k, dst, scale=1.0):
                act.wait_ge(proj_done, n + 1)
                act.activation(dst, proj[:, k, :], ACT.Copy, scale=scale).then_inc(proj_hi, 1)

            def exponentials(b, t):
                act.wait_ge(max_done, RT * b + t + 1)
                act.activation(probs[:, t % 2, :], score[t % 2][:, :, :].rearrange("p a n -> p (a n)"), ACT.Exp,
                               bias=neg_max[:, t:t + 1], accum_out=row_sum[:, t:t + 1]).then_inc(exp_done, 1)

            def probs_out(b, t):
                for half in range(2):
                    turn_out(turn0(b) + 2 * t + half, turn[:, half, :],
                             probsT[:, HI, 4 * half:4 * half + 4, t * P:(t + 1) * P])

            def sign_out(j):
                for k in range(2):
                    act.wait_ge(signs_turned, 2 * j + k + 1)
                    act.activation(signs[:, j, k, :], turn[:, k, :], ACT.Sign).then_inc(signs_ready, 1)

            def rows_out(n, r, dst):
                turn_out(n, turn[:, r % 2, :], dst[:, HI, :, r * P:(r + 1) * P])

            def batch(b, last_batch):
                n, m = turn0(b), proj0(b)
                for t in range(RT):
                    exponentials(b, t)
                    if t >= 1:
                        probs_out(b, t - 1)
                act.activation(ctx_side[:, HI], raw_ctx[:, :, :], ACT.Copy).then_inc(vals_hi, 1)
                proj_out(m, 0, new_side[:, HI, 0, :])
                proj_out(m + 1, 1, new_side[:, HI, 1, :])
                probs_out(b, RT - 1)
                proj_out(m + 2, 0, new_side[:, HI, 2, :])
                proj_out(m + 3, 1, new_side[:, HI, 3, :])
                for e in range(DC):
                    proj_out(m + 4 + e, e % 2, qT[:, HI, e, :])
                    if e in (1, 2):
                        for r in (2 * e - 2, 2 * e - 1):
                            rows_out(n + 2 * RT + r, r, xT)
                if last_batch:
                    sign_out(0)
                    sign_out(1)
                    return
                for r in range(RT):
                    rows_out(n + 3 * RT + r, r, ctx_side)
                for e in range(DC):
                    proj_out(m + 8 + e, e % 2, new_side[:, HI, e, :])
                for e in range(DC):
                    proj_out(m + 12 + e, e % 2, qT[:, HI, e, :], SCALE)

            def first_weight(w, first, r):
                turn_out(first + r, first_turn_bank(first + r), weights[:, w, HI, :, r * P:(r + 1) * P])

            for r in range(RT):
                first_weight(W_K, T_WK, r)
            for r in range(RT):
                turn_out(T_X0 + r, first_turn_bank(T_X0 + r), xT[:, HI, :, r * P:(r + 1) * P])
            for r in range(RT):
                first_weight(W_Q, T_WQ, r)
            for m in range(2 * DC):
                if m < DC:
                    proj_out(m, m % 2, new_side[:, HI, m, :])
                else:
                    proj_out(m, m % 2, qT[:, HI, m - DC, :], SCALE)
                for r in (2 * (m % 2), 2 * (m % 2) + 1):
                    if m < 2:
                        turn_out(T_C0 + r, first_turn_bank(T_C0 + r), ctx_side[:, HI, :, r * P:(r + 1) * P])
                    elif m < 4:
                        first_weight(W_V, T_WV, r)
                    elif m < 6:
                        first_weight(W_O, T_WO, r)

            with act.Fori(0, BATCH - 1) as b:
                batch(b, False)
            batch(BATCH - 1, True)

            def relu(c, j, first):
                g = HC * c + j
                if not (first and j < HR):
                    act.wait_ge(hid_ready, g - HR + 1)
                act.wait_ge(up_done, g + 1)
                act.activation(hid[:, j % HR, :], proj[:, j % 2, :], ACT.Relu,
                               scale=hid_gain[:, j:j + 1]).then_inc(relu_done, 1)

            def ffn_block(c, nxt, first, last_block):
                for j in range(HC):
                    if first and j + 2 < HC:
                        sign_out(j + 2)
                    relu(c, j, first)
                    if first and j >= HC - 2:
                        for r in (2 * (j - HC + 2), 2 * (j - HC + 2) + 1):
                            rows_out(TURNS_ALL + r, r, four_x[:, nxt])
                    if not first and not last_block and 8 <= j < 12:
                        rows_out(TURNS_ALL + RT * c + j - 8, j - 8, four_x[:, nxt])

            ffn_block(0, 1, True, False)
            with act.Fori(1, BATCH - 1) as c:
                ffn_block(c, c + 1, False, False)
            ffn_block(BATCH - 1, 0, False, True)

        @block.vector
        def _(dve):
            def four(bank):
                return bank.rearrange("p (k n) -> p k n", n=P)

            def turn_out(n, bank, dst):
                dve.wait_ge(turn_hi, n + 1)
                dve.tensor_tensor(dst(LO), four(bank), dst(HI).bitcast(F32), ALU.subtract).then_inc(turn_lo, 1)

            def proj_out(n, k, dst, scale=None):
                dve.wait_ge(proj_hi, n + 1)
                if scale is None:
                    dve.tensor_tensor(dst(LO), proj[:, k, :], dst(HI).bitcast(F32), ALU.subtract
                                      ).then_inc(proj_lo, 1)
                else:
                    dve.scalar_tensor_tensor(dst(LO), proj[:, k, :], scale, dst(HI).bitcast(F32),
                                             ALU.mult, ALU.subtract).then_inc(proj_lo, 1)

            def chunk(buf, c):
                return lambda s: buf[:, s, c, :]

            def part(buf, r):
                return lambda s: buf[:, s, :, r * P:(r + 1) * P]

            def maxima(b, t):
                dve.wait_ge(scored, RT * b + t + 1)
                dve.reduce_max(neg_max[:, t:t + 1], score[t % 2][:, :, :].rearrange("p a n -> p (a n)"),
                               AX.X, negate=True).then_inc(max_done, 1)

            def probs_out(b, t):
                for half in range(2):
                    turn_out(turn0(b) + 2 * t + half, turn[:, half, :],
                             lambda s, half=half: probsT[:, s, 4 * half:4 * half + 4, t * P:(t + 1) * P])

            def norm_stats(n, tile0):
                for r in range(RT):
                    dve.bn_stats(stats[:, r, :], rows[:, tile0 + r, :]).then_inc(stats_done, 1)

            def norm_moments(n):
                for r in range(RT):
                    dve.bn_aggr(mean_var[:, r, :], stats[:, r, :]).then_inc(meanvar_done, 1)

            def norm_rows(n, tile0):
                dve.wait_ge(rstd_done, n + 1)
                for r in range(RT):
                    dve.tensor_scalar(normed[:, r, :], rows[:, tile0 + r, :], mean_var[:, r, 0:1], rstd[:, r:r + 1],
                                      ALU.subtract, ALU.mult).then_inc(normed_done, 1)

            def batch(b, next_tile0, last_batch):
                n, m = turn0(b), proj0(b)
                maxima(b, 0)
                maxima(b, 1)
                probs_out(b, 0)
                if not last_batch:
                    dve.wait_ge(xrest_in, 16 * (BATCH - 1))
                norm_stats(b + 1, next_tile0)
                dve.wait_ge(stats_done, RT * (b + 1) + RT)
                maxima(b, 2)
                norm_moments(b + 1)
                probs_out(b, 1)
                maxima(b, 3)
                probs_out(b, 2)
                norm_rows(b + 1, next_tile0)
                proj_out(m, 0, chunk(new_side, 0))
                proj_out(m + 1, 1, chunk(new_side, 1))
                probs_out(b, 3)
                proj_out(m + 2, 0, chunk(new_side, 2))
                proj_out(m + 3, 1, chunk(new_side, 3))
                dve.wait_ge(exp_done, RT * b + RT)
                dve.reciprocal(row_inv[:, :], row_sum[:, :]).then_inc(inv_done, 1)
                dve.wait_ge(inv_done, b + 1)
                dve.tensor_scalar(row_gain[:, :], row_inv[:, :], gates[:, 0:1], None, ALU.mult
                                  ).then_inc(rowgain_done, 1)
                for e in range(DC):
                    proj_out(m + 4 + e, e % 2, chunk(qT, e))
                    if e in (1, 2):
                        for r in (2 * e - 2, 2 * e - 1):
                            turn_out(n + 2 * RT + r, turn[:, r % 2, :], part(xT, r))
                if not last_batch:
                    for r in range(RT):
                        turn_out(n + 3 * RT + r, turn[:, r % 2, :], part(ctx_side, r))
                dve.wait_ge(rowgain_done, b + 1)
                for r in range(RT):
                    dve.wait_ge(wo_done, RT * b + r + 1)
                    mine = rows[:, RT * b + r, :]
                    dve.scalar_tensor_tensor(mine, wide(r), row_gain[:, r:r + 1], mine, ALU.mult, ALU.add
                                             ).then_inc(attended, 1)
                if last_batch:
                    return
                for e in range(DC):
                    proj_out(m + 8 + e, e % 2, chunk(new_side, e))
                for e in range(DC):
                    proj_out(m + 12 + e, e % 2, chunk(qT, e), SCALE)

            dve.wait_ge(x0_in, 16)
            norm_stats(0, 0)
            dve.wait_ge(stats_done, RT)
            norm_moments(0)
            for r in range(RT):
                turn_out(T_WK + r, first_turn_bank(T_WK + r), part(weights[:, W_K], r))
            norm_rows(0, 0)
            for r in range(RT):
                turn_out(T_X0 + r, first_turn_bank(T_X0 + r), part(xT, r))
            for r in range(RT):
                turn_out(T_WQ + r, first_turn_bank(T_WQ + r), part(weights[:, W_Q], r))
            for m in range(2 * DC):
                if m < DC:
                    proj_out(m, m % 2, chunk(new_side, m))
                else:
                    proj_out(m, m % 2, chunk(qT, m - DC), SCALE)
                for r in (2 * (m % 2), 2 * (m % 2) + 1):
                    if m < 2:
                        turn_out(T_C0 + r, first_turn_bank(T_C0 + r), part(ctx_side, r))
                    elif m < 4:
                        turn_out(T_WV + r, first_turn_bank(T_WV + r), part(weights[:, W_V], r))
                    elif m < 6:
                        turn_out(T_WO + r, first_turn_bank(T_WO + r), part(weights[:, W_O], r))
            dve.wait_ge(tanh_done, 1)
            dve.tensor_tensor(ffn_gain[:, :], gates[:, 1:2], gates_raw[:, 2:3], ALU.mult).then_inc(gain_done, 1)
            dve.wait_ge(gain_done, 1)
            dve.tensor_scalar(out_gain[:, :], out_gain[:, :], ffn_gain[:, 0:1], None, ALU.mult
                              ).then_inc(gain_done, 1)

            with dve.Fori(0, BATCH - 1) as b:
                batch(b, RT * b + RT, False)
            batch(BATCH - 1, 0, True)

            def split_hidden(c, j, first):
                g = HC * c + j
                slot = hid_split[:, j % HR]
                dve.wait_ge(relu_done, g + 1)
                if not (first and j < HR):
                    dve.wait_ge(down_done, RT * (g - HR + 1))
                dve.tensor_copy(slot[:, HI, :], hid[:, j % HR, :]).then_inc(hid_hi, 1)
                dve.wait_ge(hid_hi, g + 1)
                dve.tensor_tensor(slot[:, LO, :], hid[:, j % HR, :], slot[:, HI, :].bitcast(F32), ALU.subtract
                                  ).then_inc(hid_ready, 1)

            def finish_tile(c, r):
                dve.wait_ge(down_done, RT * (HC * c + HC - 1) + r + 1)
                dve.tensor_tensor(spare[:, r % 2, :], wide(r), out_gain[:, :], ALU.mult).then_inc(acc_free, 1)
                dve.wait_ge(acc_free, RT * c + r + 1)
                mine = rows[:, RT * c + r, :]
                dve.tensor_tensor(mine, mine, spare[:, r % 2, :], ALU.add).then_inc(out_ready, 1)

            def ffn_block(c, nxt, first, last_block):
                for j in range(HC):
                    if not last_block and j == 4:
                        dve.wait_ge(stats_done, RT * (BATCH + c + 2))
                    split_hidden(c, j, first)
                    if not last_block and j == 4:
                        norm_moments(BATCH + c + 1)
                    if not first and j == 1:
                        for r in range(RT):
                            finish_tile(c - 1, r)
                    if not last_block and j == 3:
                        norm_stats(BATCH + c + 1, RT * c + RT)
                    if not last_block and j == 6:
                        norm_rows(BATCH + c + 1, RT * c + RT)
                    if first and j >= HC - 2:
                        for r in (2 * (j - HC + 2), 2 * (j - HC + 2) + 1):
                            turn_out(TURNS_ALL + r, turn[:, r % 2, :], part(four_x[:, nxt], r))
                    if not first and not last_block and 8 <= j < 12:
                        turn_out(TURNS_ALL + RT * c + j - 8, turn[:, (j - 8) % 2, :], part(four_x[:, nxt], j - 8))

            ffn_block(0, 1, True, False)
            with dve.Fori(1, BATCH - 1) as c:
                ffn_block(c, c + 1, False, False)
            ffn_block(BATCH - 1, 0, False, True)
            for r in range(RT):
                finish_tile(BATCH - 1, r)


_INS = ['x', 'ctx_2048', 'g_xattn', 'g_ffn', 'L0_xattn_wq', 'L0_xattn_wk', 'L0_xattn_wv', 'L0_xattn_wo',
        'L0_ffn_up_weight', 'L0_ffn_down_weight', 'L0_ffn_up_scale', 'L0_ffn_down_scale', 'L0_ffn_output_scale']


def kernel(**inputs):
    import numpy as _np
    import concourse.bacc as _bacc
    from concourse import mybir as _mybir
    from concourse.bass_utils import run_bass_kernel_spmd as _run

    nc = _bacc.Bacc("TRN2", target_bir_lowering=False, num_devices=1, dynamic_dma_scratch_size=256)
    arrays, args = {}, []
    for name in _INS:
        a = _np.ascontiguousarray(inputs[name])
        arrays[f"in_{name}"] = a
        args.append(nc.dram_tensor(f"in_{name}", a.shape, _mybir.dt.from_np(a.dtype), kind="ExternalInput").ap())
    shape = inputs['x'].shape
    args.append(nc.dram_tensor("result", tuple(shape), _mybir.dt.float32, kind="ExternalOutput").ap())
    gated_block(nc, *args)
    r = _run(nc, [arrays], core_ids=[0])
    return r.results[0]["result"]
```

```python
from contextlib import ExitStack

import concourse.bass as bass
from concourse import mybir

F32 = mybir.dt.float32
F32R = mybir.dt.float32r
BF16 = mybir.dt.bfloat16
ALU = mybir.AluOpType
ACT = mybir.ActivationFunctionType
AX = mybir.AxisListType

P = 128
HI, LO = 0, 1
PASSES = ((HI, HI), (HI, LO), (LO, HI))


def gated_block(nc, x, ctx_kv, g_xattn, g_ffn, wq, wk, wv, wo, up_w, down_w, up_scale, down_scale,
                output_scale, out):
    BATCH, ROWS, DIM = x.shape
    HIDDEN = up_w.shape[0]
    RT = ROWS // P
    DC = DIM // P
    KEYS = ctx_kv.shape[1] + ROWS
    KC = KEYS // P
    HC = HIDDEN // P
    EPS = 1e-5
    SCALE = float(DIM) ** -0.5
    assert RT == 4 and DC == 4 and KC == 8 and HC == 16 and BATCH == 4

    W_K, W_Q, W_V, W_O = range(4)
    TURNS_FIRST = 4 * RT + RT + RT
    TURNS_BATCH = 2 * RT + RT + RT
    TURNS_ALL = TURNS_FIRST + TURNS_BATCH * (BATCH - 1) + 3 * RT
    PROJS_FIRST = 2 * DC
    PROJS_BATCH = 4 * 4
    PROJS_ALL = PROJS_FIRST + PROJS_BATCH * (BATCH - 1) + 2 * 4
    T_WK, T_X0, T_WQ, T_C0, T_WV, T_WO = (RT * i for i in range(6))

    BETWEEN = (2, 2, 2, 3, 3, 2, 2, 0)
    assert len(BETWEEN) == PROJS_FIRST and T_WQ + sum(BETWEEN) == TURNS_FIRST

    def turns_after(m):
        first = T_WQ + sum(BETWEEN[:m])
        return range(first, first + BETWEEN[m])

    def turn0(b):
        return TURNS_FIRST + TURNS_BATCH * b

    def proj0(b):
        return PROJS_FIRST + PROJS_BATCH * b

    row_tiles = "(r p) d -> p r d"
    x_v = x.rearrange("b (r p) d -> b p r d", p=P)
    ctx_v = ctx_kv.rearrange("b (r p) d -> b p r d", p=P)
    out_v = out.rearrange("b (r p) d -> p (b r) d", p=P)
    up_v = up_w.rearrange("(j p) d -> j p d", p=P)
    down_v = down_w.rearrange("(r p) (j h) -> j p r h", p=P, h=P)

    with ExitStack() as stack:
        def sb(name, shape, dt=F32):
            return stack.enter_context(nc.sbuf_tensor(name, shape, dt))

        def pb(name, shape):
            return stack.enter_context(nc.psum_tensor(name, shape, F32))

        def sem(name):
            return stack.enter_context(nc.semaphore(name))

        rows = sb("rows", [P, BATCH * RT, DIM])
        weights = sb("weights", [P, 4, 2, DC, DIM], F32R)
        four_x = sb("four_x", [P, 4, 2, DC, ROWS], F32R)
        xT, qT = four_x[:, 0], four_x[:, 1]
        ctx_side = four_x[:, 2]
        new_side = four_x[:, 3]
        probsT = sb("probsT", [P, 2, KC, ROWS], F32R)
        probs = sb("probs", [P, 2, KEYS])
        raw_ctx = sb("raw_ctx", [P, RT, DIM])
        normed = sb("normed", [P, RT, DIM])
        plain_signs = sb("plain_signs", [P, 2, 2, DIM], BF16)
        out_gain = sb("out_gain", [P, DIM])
        ident = sb("ident", [P, P])
        ident16 = sb("ident16", [P, P], BF16)
        hid_gain = sb("hid_gain", [P, HC])
        stats = sb("stats", [P, RT, 6])
        mean_var = sb("mean_var", [P, RT, 2])
        var_eps = sb("var_eps", [P, RT])
        minus_half = sb("minus_half", [P, RT])
        eps = sb("eps", [P, RT])
        rstd = sb("rstd", [P, RT])
        neg_max = sb("neg_max", [P, RT])
        row_sum = sb("row_sum", [P, RT])
        row_inv = sb("row_inv", [P, RT])
        row_gain = sb("row_gain", [P, RT])
        gates_raw = sb("gates_raw", [P, 3])
        gates = sb("gates", [P, 2])
        ffn_gain = sb("ffn_gain", [P, 1])

        signs = weights[:, :, :, :, :].rearrange("p w s c n -> p (w s c n)").rearrange(
            "p (j k n) -> p j k n", j=HC, k=2)
        raw_signs = raw_ctx[:, :, :].rearrange("p (s k) n -> p s k n", s=2)
        hid = probs[:, :, :].rearrange("p s (k n) -> p (s k) n", n=ROWS)
        scaled = raw_ctx
        HR = 4
        hid_split = probsT[:, :, :, :].rearrange("p s k n -> p (s k) n").rearrange(
            "p (k s) n -> p k s n", s=2)

        score = [pb(f"score{i}", [P, 2, 512]) for i in range(2)]
        proj = pb("proj", [P, 2, 512])
        turn = pb("turn", [P, 2, 512])

        def wide(r):
            return score[r // 2][:, r % 2, :]

        def first_turn_bank(n):
            k = n % 6
            return turn[:, k, :] if k < 2 else wide(k - 2)

        small_in, xrest_in, ctx_in, out_stored = map(sem, ("small_in", "xrest_in", "ctx_in", "out_stored"))
        x0_in = [sem(f"x0_in{i}") for i in range(RT)]
        wk_in = [sem(f"wk_in{i}") for i in range(RT)]
        w_in = {w: sem(f"w_in{w}") for w in (W_Q, W_V, W_O)}
        signs_in = [sem(f"signs_in{i}") for i in range(2)]
        ident_zero, ident_ready, half_ready = map(sem, ("ident_zero", "ident_ready", "half_ready"))
        tanh_done, gain_done = sem("tanh_done"), sem("gain_done")
        turned, turn_hi, turn_lo = map(sem, ("turned", "turn_hi", "turn_lo"))
        proj_done, proj_hi, proj_lo = map(sem, ("proj_done", "proj_hi", "proj_lo"))
        scored, max_done, exp_done = map(sem, ("scored", "max_done", "exp_done"))
        vals_hi, vals_ready = sem("vals_hi"), sem("vals_ready")
        stats_done, meanvar_done, eps_done, rstd_done, normed_done = map(sem, (
            "stats_done", "meanvar_done", "eps_done", "rstd_done", "normed_done"))
        inv_done, rowgain_done = sem("inv_done"), sem("rowgain_done")
        wo_done, attended = sem("wo_done"), sem("attended")
        signs_plain, signs_turned, signs_ready = map(sem, ("signs_plain", "signs_turned", "signs_ready"))
        up_done, relu_done, hid_hi, hid_ready = map(sem, ("up_done", "relu_done", "hid_hi", "hid_ready"))
        down_done, acc_out, acc_scaled, out_ready = map(sem, ("down_done", "acc_out", "acc_scaled", "out_ready"))

        odd_scaled, pool_scaled, pool_out_ready = map(sem, ("odd_scaled", "pool_scaled", "pool_out_ready"))
        last_scaled = sem("last_scaled")
        LAST = RT * (BATCH - 1)
        LAST_DOWNS = [(j, r) for r in (0, 1) for j in (HC - 3, HC - 2)] + [(HC - 1, 0), (HC - 1, 1)] + [
            (j, r) for r in (2, 3) for j in (HC - 3, HC - 2, HC - 1)]

        def last_down(r):
            return RT * (HC * BATCH - 3) + LAST_DOWNS.index((HC - 1, r)) + 1

        LAST_POOL, LAST_DVE = 1, (0, 2, 3)

        block = stack.enter_context(nc.Block())

        @block.sync
        def _(sp):
            for r in range(RT):
                sp.dma_start(rows[:, r, :], x_v[0, :, r, :]).then_inc(x0_in[r], 16)
            for r in range(RT):
                sp.dma_start(rows[:, RT + r, :], wk[r * P:(r + 1) * P, :]).then_inc(wk_in[r], 16)
            sp.dma_start(raw_ctx[:, :, :], ctx_v[0]).then_inc(ctx_in, 16)
            sp.dma_start(rows[:, RT * 2:RT * 3, :], wq.rearrange(row_tiles, p=P)).then_inc(w_in[W_Q], 16)
            sp.dma_start(rows[:, RT * 3:RT * 4, :], wv.rearrange(row_tiles, p=P)).then_inc(w_in[W_V], 16)
            sp.dma_start(probs[:, :, :].rearrange("p s (k n) -> p (s k) n", n=DIM),
                         wo.rearrange(row_tiles, p=P)).then_inc(w_in[W_O], 16)
            for i, g in enumerate((g_xattn, g_ffn, output_scale)):
                sp.dma_start(gates_raw[:, i:i + 1], g.rearrange("(a n) -> a n", a=1).broadcast_to([P, 1])
                             ).then_inc(small_in, 16)
            sp.dma_start(out_gain[:, :], down_scale.rearrange("(a n) -> a n", a=1).broadcast_to([P, DIM])
                         ).then_inc(small_in, 16)
            with nc.allow_non_contiguous_dma("2048 scales, once"):
                sp.dma_start(hid_gain[:, :], up_scale.rearrange("(j p) -> p j", p=P)).then_inc(small_in, 16)
            for b, last_turn in ((1, T_WK), (2, T_WQ), (3, T_WV)):
                sp.wait_ge(turned, last_turn + RT)
                sp.dma_start(rows[:, RT * b:RT * (b + 1), :], x_v[b]).then_inc(xrest_in, 16)
            with sp.Fori(0, BATCH - 1) as b:
                sp.wait_ge(vals_ready, b + 1)
                sp.dma_start(raw_ctx[:, :, :], ctx_v[b + 1]).then_inc(ctx_in, 16)
            sp.wait_ge(vals_ready, BATCH)
            for j in range(HC):
                if j >= 2:
                    sp.wait_ge(signs_plain, j - 1)
                sp.dma_start(raw_signs[:, j % 2, 0, :], up_v[j]).then_inc(signs_in[j % 2], 16)
                sp.dma_start(raw_signs[:, j % 2, 1, :].rearrange("p (r h) -> p r h", h=P), down_v[j]
                             ).then_inc(signs_in[j % 2], 16)
            with sp.Fori(0, BATCH * RT - RT) as t:
                sp.wait_ge(out_ready, t + 1)
                sp.dma_start(out_v[:, t, :], rows[:, t, :]).then_inc(out_stored, 16)
            for r in (0, 2, LAST_POOL, 3):
                if r == LAST_POOL:
                    sp.wait_ge(pool_out_ready, 1)
                else:
                    sp.wait_ge(out_ready, RT * (BATCH - 1) + LAST_DVE.index(r) + 1)
                sp.dma_start(out_v[:, LAST + r, :], rows[:, LAST + r, :]).then_inc(out_stored, 16)
            sp.wait_ge(out_stored, 16 * BATCH * RT)

        @block.gpsimd
        def _(pool):
            pool.memset(ident[:, :], 0.0).then_inc(ident_zero, 1)
            pool.memset(minus_half[:, :], -0.5).then_inc(half_ready, 1)
            pool.memset(eps[:, :], EPS).then_inc(half_ready, 1)
            pool.wait_ge(ident_zero, 1)
            pool.affine_select(out=ident[:, :], in_=ident[:, :], compare_op=ALU.not_equal, fill=1.0, base=0,
                               pattern=[[-1, P]], channel_multiplier=1).then_inc(ident_ready, 1)
            pool.wait_ge(ident_ready, 1)
            pool.tensor_copy(ident16[:, :], ident[:, :]).then_inc(ident_ready, 1)
            pool.wait_ge(half_ready, 2)

            def inverse_std(n):
                pool.wait_ge(meanvar_done, RT * n + RT)
                pool.tensor_tensor(var_eps[:, :], mean_var[:, :, 1], eps[:, :], ALU.add).then_inc(eps_done, 1)
                pool.wait_ge(eps_done, n + 1)
                pool.tensor_tensor(rstd[:, :], var_eps[:, :], minus_half[:, :], ALU.pow).then_inc(rstd_done, 1)

            def batch(b):
                inverse_std(b + 1)
                pool.wait_ge(vals_hi, b + 1)
                pool.tensor_tensor(ctx_side[:, LO], raw_ctx[:, :, :], ctx_side[:, HI].bitcast(F32),
                                   ALU.subtract).then_inc(vals_ready, 1)

            inverse_std(0)
            with pool.Fori(0, BATCH) as b:
                batch(b)
            for n in range(BATCH + 1, 2 * BATCH):
                inverse_std(n)
            pool.wait_ge(acc_out, 2 * (BATCH - 1) + 1)
            pool.tensor_tensor(scaled[:, LAST_POOL, :], scaled[:, LAST_POOL, :], out_gain[:, :], ALU.mult
                               ).then_inc(pool_scaled, 1)
            pool.wait_ge(pool_scaled, 1)
            pool.tensor_tensor(rows[:, LAST + LAST_POOL, :], rows[:, LAST + LAST_POOL, :], scaled[:, LAST_POOL, :],
                               ALU.add).then_inc(pool_out_ready, 1)

        @block.tensor
        def _(pe):
            def transposes(bank, tiles, done):
                for k, tile in enumerate(tiles):
                    last = pe.transpose(bank[:, k * P:(k + 1) * P], tile, ident[:, :])
                last.then_inc(done, 1)

            def turn_job(n, k, tiles):
                pe.wait_ge(turn_lo, n - 1)
                transposes(turn[:, k, :], tiles, turned)

            def cols(src):
                return [src[:, k * P:(k + 1) * P] for k in range(4)]

            def product(bank, lhs, rhs, start, stop):
                for i, (l, r) in enumerate(PASSES):
                    last = pe.matmul(bank, lhs(l), rhs(r), start=start and i == 0, stop=stop and i == 2)
                return last

            def proj_job(n, k, terms, bank_unused=False):
                if not bank_unused:
                    pe.wait_ge(proj_lo, n - 1)
                for i, (lhs, rhs) in enumerate(terms):
                    last = product(proj[:, k, :], lhs, rhs, i == 0, i == len(terms) - 1)
                last.then_inc(proj_done, 1)

            def out_of(buf, c, lo, hi):
                return lambda s: buf[:, s, c, lo:hi]

            def feature_major(w, e):
                return [(out_of(weights[:, w], c, e * P, (e + 1) * P), out_of(xT, c, 0, ROWS)) for c in range(DC)]

            def v_terms(r):
                return [(out_of(xT, c, r * P, (r + 1) * P), out_of(weights[:, W_V], c, 0, DIM)) for c in range(DC)]

            def attn_terms(e):
                new = [(out_of(new_side, r, e * P, (e + 1) * P), out_of(probsT, DC + r, 0, ROWS)) for r in range(RT)]
                old = [(out_of(ctx_side, r, e * P, (e + 1) * P), out_of(probsT, r, 0, ROWS)) for r in range(RT)]
                return new, old

            def scores(b, t):
                if t >= 2:
                    pe.wait_ge(exp_done, RT * b + t - 1)
                for half, side in enumerate((ctx_side, new_side)):
                    for c in range(DC):
                        if t == 0 and half == 0:
                            pe.wait_ge(proj_lo, proj0(b) - DC + c + 1)
                        last = product(score[t % 2][:, half, :], out_of(qT, c, t * P, (t + 1) * P),
                                       out_of(side, c, 0, ROWS), c == 0, c == DC - 1)
                last.then_inc(scored, 1)

            def turn_probs(b, t):
                pe.wait_ge(exp_done, RT * b + t + 1)
                for half in range(2):
                    turn_job(turn0(b) + 2 * t + half, half, cols(probs[:, t % 2, half * 512:(half + 1) * 512]))

            def turn_next_rows(b, r):
                pe.wait_ge(normed_done, RT * (b + 1) + r + 1)
                turn_job(turn0(b) + 2 * RT + r, r % 2, cols(normed[:, r, :]))

            def turn_next_context(b, r):
                if r == 0:
                    pe.wait_ge(ctx_in, 16 * (b + 2))
                turn_job(turn0(b) + 3 * RT + r, r % 2, cols(raw_ctx[:, r, :]))

            def turn_signs(j):
                pe.wait_ge(signs_plain, j + 1)
                if j < 2:
                    pe.wait_ge(turn_lo, TURNS_ALL)
                else:
                    pe.wait_ge(signs_ready, j - 1)
                bank = turn[:, j % 2, :].bitcast(BF16)
                for k in range(2):
                    for i in range(4):
                        last = pe.transpose(bank[:, k * DIM + i * P:k * DIM + (i + 1) * P],
                                            plain_signs[:, j % 2, k, i * P:(i + 1) * P], ident16[:, :])
                last.then_inc(signs_turned, 1)

            def batch(b, last_batch):
                for t in range(RT):
                    scores(b, t)
                    if t >= 1:
                        turn_probs(b, t - 1)
                n = proj0(b)
                proj_job(n, 0, v_terms(0))
                proj_job(n + 1, 1, v_terms(1))
                turn_probs(b, RT - 1)
                proj_job(n + 2, 0, v_terms(2))
                proj_job(n + 3, 1, v_terms(3))
                pe.wait_ge(turn_lo, turn0(b) + 2 * RT)
                for e in range(DC):
                    new, old = attn_terms(e)
                    pe.wait_ge(proj_lo, n + 4 + e - 1)
                    for i, (lhs, rhs) in enumerate(new):
                        if e == 0:
                            pe.wait_ge(proj_lo, n + i + 1)
                        product(proj[:, e % 2, :], lhs, rhs, i == 0, False)
                    if e == 0:
                        pe.wait_ge(vals_ready, b + 1)
                    for i, (lhs, rhs) in enumerate(old):
                        last = product(proj[:, e % 2, :], lhs, rhs, False, i == RT - 1)
                    last.then_inc(proj_done, 1)
                    if e in (1, 2):
                        turn_next_rows(b, 2 * (e - 1))
                        turn_next_rows(b, 2 * (e - 1) + 1)
                for c in range(DC):
                    pe.wait_ge(proj_lo, n + 4 + c + 1)
                    for r in range(RT):
                        if c == 0 and r in (0, 2):
                            pe.wait_ge(exp_done, RT * b + RT)
                        last = product(wide(r), out_of(qT, c, r * P, (r + 1) * P),
                                       out_of(weights[:, W_O], c, 0, DIM), c == 0, c == DC - 1)
                        if c == DC - 1:
                            last.then_inc(wo_done, 1)
                    if c < 2 and not last_batch:
                        turn_next_context(b, 2 * c)
                        turn_next_context(b, 2 * c + 1)
                    if c < 2 and last_batch:
                        turn_signs(c)
                if not last_batch:
                    pe.wait_ge(turn_lo, turn0(b) + 3 * RT)
                    for e in range(DC):
                        proj_job(n + 8 + e, e % 2, feature_major(W_K, e))
                    for e in range(DC):
                        if e == DC - 1:
                            pe.wait_ge(attended, RT * (b + 1))
                            pe.wait_ge(turn_lo, turn0(b + 1))
                        proj_job(n + 12 + e, e % 2, feature_major(W_Q, e))

            def first_turn(n, tiles):
                if n >= 6:
                    pe.wait_ge(turn_lo, n - 5)
                transposes(first_turn_bank(n), tiles, turned)

            def first_weight(w, first, buf, r):
                if w == W_K:
                    pe.wait_ge(wk_in[r], 16)
                elif r == 0:
                    pe.wait_ge(w_in[w], 16)
                first_turn(first + r, cols(buf[:, r, :]))

            wo_raw = probs[:, :, :].rearrange("p s (k n) -> p (s k) n", n=DIM)
            pe.wait_ge(ident_ready, 2)
            for r in range(RT):
                first_weight(W_K, T_WK, rows[:, RT * 1:RT * 2, :], r)
            for r in range(RT):
                pe.wait_ge(normed_done, r + 1)
                first_turn(T_X0 + r, cols(normed[:, r, :]))
            pe.wait_ge(turn_lo, T_X0 + RT)
            for m in range(2 * DC):
                if m == DC:
                    pe.wait_ge(turn_lo, T_WQ + RT)
                proj_job(m, m % 2, feature_major(W_K if m < DC else W_Q, m % DC), bank_unused=m < 2)
                for n in turns_after(m):
                    if n < T_C0:
                        first_weight(W_Q, T_WQ, rows[:, RT * 2:RT * 3, :], n - T_WQ)
                    elif n < T_WV:
                        if n == T_C0:
                            pe.wait_ge(ctx_in, 16)
                        first_turn(n, cols(raw_ctx[:, n - T_C0, :]))
                    elif n < T_WO:
                        first_weight(W_V, T_WV, rows[:, RT * 3:RT * 4, :], n - T_WV)
                    else:
                        first_weight(W_O, T_WO, wo_raw, n - T_WO)
            pe.wait_ge(turn_lo, TURNS_FIRST)

            with pe.Fori(0, BATCH - 1) as b:
                batch(b, False)
            batch(BATCH - 1, True)

            def up(c, j, src, first):
                g = HC * c + j
                if first:
                    pe.wait_ge(signs_ready, j + 1)
                if first and j < 2:
                    pe.wait_ge(proj_lo, PROJS_ALL)
                else:
                    pe.wait_ge(relu_done, g - 1)
                for k in range(DC):
                    for s in (HI, LO):
                        last = pe.matmul(proj[:, j % 2, :], signs[:, j, 0, k * P:(k + 1) * P], src(s, k),
                                         start=(k == 0 and s == HI), stop=(k == DC - 1 and s == LO))
                last.then_inc(up_done, 1)

            def down(c, j, first=False, tiles=range(RT)):
                g = HC * c + j
                pe.wait_ge(hid_ready, g + 1)
                for r in tiles:
                    if j == 0 and first:
                        pe.wait_ge(attended, RT * (BATCH - 1) + r + 1)
                    elif j == 0:
                        pe.wait_ge(acc_out if r % 2 else acc_scaled, 2 * (c - 1) + r // 2 + 1)
                    for s in (HI, LO):
                        last = pe.matmul(wide(r), hid_split[:, j % HR, s, r * P:(r + 1) * P], signs[:, j, 1, :],
                                         start=(j == 0 and s == HI), stop=(j == HC - 1 and s == LO))
                    last.then_inc(down_done, 1)

            def turn_next_block(c, r, src):
                pe.wait_ge(normed_done, RT * (BATCH + c + 1) + r + 1)
                turn_job(TURNS_ALL + RT * c + r, r % 2, cols(src[:, r, :]))

            def ffn_block(c, cur, first, last_block):
                pe.wait_ge(turn_lo, TURNS_ALL + RT * c)
                for j in range(HC):
                    if first and j + 2 < HC:
                        turn_signs(j + 2)
                    up(c, j, lambda s, k: four_x[:, cur, s, k, :], first)
                    if first and j >= HC - 2:
                        if j == HC - 2:
                            pe.wait_ge(signs_ready, HC)
                        turn_next_block(c, 2 * (j - HC + 2), normed)
                        turn_next_block(c, 2 * (j - HC + 2) + 1, normed)
                    if first and j >= 2:
                        down(c, j - 2, True)
                    if not first and not (last_block and j == HC - 1):
                        down(c - 1, HC - 2 + j) if j < 2 else down(c, j - 2)
                    if not first and not last_block and 8 <= j < 12:
                        turn_next_block(c, j - 8, normed)

            ffn_block(0, 0, True, False)
            with pe.Fori(1, BATCH - 1) as c:
                ffn_block(c, c, False, False)
            ffn_block(BATCH - 1, BATCH - 1, False, True)
            for j, r in LAST_DOWNS:
                down(BATCH - 1, j, tiles=[r])

        @block.scalar
        def _(act):
            def four(bank):
                return bank.rearrange("p (k n) -> p k n", n=P)

            def turn_out(n, bank, dst):
                act.wait_ge(turned, n + 1)
                act.activation(dst, four(bank), ACT.Copy).then_inc(turn_hi, 1)

            def proj_out(n, k, dst, scale=1.0):
                act.wait_ge(proj_done, n + 1)
                act.activation(dst, proj[:, k, :], ACT.Copy, scale=scale).then_inc(proj_hi, 1)

            def exponentials(b, t):
                act.wait_ge(max_done, RT * b + t + 1)
                act.activation(probs[:, t % 2, :], score[t % 2][:, :, :].rearrange("p a n -> p (a n)"), ACT.Exp,
                               bias=neg_max[:, t:t + 1], accum_out=row_sum[:, t:t + 1]).then_inc(exp_done, 1)

            def probs_out(b, t):
                for half in range(2):
                    turn_out(turn0(b) + 2 * t + half, turn[:, half, :],
                             probsT[:, HI, 4 * half:4 * half + 4, t * P:(t + 1) * P])

            def take_signs(j):
                if j >= 2:
                    act.wait_ge(signs_turned, j - 1)
                act.wait_ge(signs_in[j % 2], 32 * (j // 2 + 1))
                act.activation(plain_signs[:, j % 2], raw_signs[:, j % 2], ACT.Sign).then_inc(signs_plain, 1)

            def rows_out(n, r, dst):
                turn_out(n, turn[:, r % 2, :], dst[:, HI, :, r * P:(r + 1) * P])

            def batch(b, last_batch):
                n, m = turn0(b), proj0(b)
                for t in range(RT):
                    exponentials(b, t)
                    if t >= 1:
                        probs_out(b, t - 1)
                act.activation(ctx_side[:, HI], raw_ctx[:, :, :], ACT.Copy).then_inc(vals_hi, 1)
                proj_out(m, 0, new_side[:, HI, 0, :])
                proj_out(m + 1, 1, new_side[:, HI, 1, :])
                probs_out(b, RT - 1)
                proj_out(m + 2, 0, new_side[:, HI, 2, :])
                proj_out(m + 3, 1, new_side[:, HI, 3, :])
                for e in range(DC):
                    proj_out(m + 4 + e, e % 2, qT[:, HI, e, :])
                    if e in (1, 2):
                        for r in (2 * e - 2, 2 * e - 1):
                            rows_out(n + 2 * RT + r, r, xT)
                if last_batch:
                    for j in range(4):
                        take_signs(j)
                    return
                for r in range(RT):
                    rows_out(n + 3 * RT + r, r, ctx_side)
                for e in range(DC):
                    proj_out(m + 8 + e, e % 2, new_side[:, HI, e, :])
                for e in range(DC):
                    proj_out(m + 12 + e, e % 2, qT[:, HI, e, :], SCALE)

            def first_weight(w, first, r):
                turn_out(first + r, first_turn_bank(first + r), weights[:, w, HI, :, r * P:(r + 1) * P])

            for r in range(RT):
                first_weight(W_K, T_WK, r)
            for r in range(RT):
                turn_out(T_X0 + r, first_turn_bank(T_X0 + r), xT[:, HI, :, r * P:(r + 1) * P])
            for m in range(2 * DC):
                if m < DC:
                    proj_out(m, m % 2, new_side[:, HI, m, :])
                else:
                    proj_out(m, m % 2, qT[:, HI, m - DC, :], SCALE)
                for n in turns_after(m):
                    if n < T_C0:
                        first_weight(W_Q, T_WQ, n - T_WQ)
                    elif n < T_WV:
                        r = n - T_C0
                        turn_out(n, first_turn_bank(n), ctx_side[:, HI, :, r * P:(r + 1) * P])
                    elif n < T_WO:
                        first_weight(W_V, T_WV, n - T_WV)
                    else:
                        first_weight(W_O, T_WO, n - T_WO)

            act.wait_ge(small_in, 16 * 5)
            act.activation(gates[:, :], gates_raw[:, 0:2], ACT.Tanh).then_inc(tanh_done, 1)
            with act.Fori(0, BATCH - 1) as b:
                batch(b, False)
            batch(BATCH - 1, True)

            def relu(c, j, first):
                g = HC * c + j
                if not (first and j < HR):
                    act.wait_ge(hid_ready, g - HR + 1)
                act.wait_ge(up_done, g + 1)
                act.activation(hid[:, j % HR, :], proj[:, j % 2, :], ACT.Relu,
                               scale=hid_gain[:, j:j + 1]).then_inc(relu_done, 1)

            def accumulator_out(c, r):
                act.wait_ge(down_done, RT * (HC * c + HC - 1) + r + 1)
                act.activation(scaled[:, r, :], wide(r), ACT.Copy).then_inc(acc_out, 1)

            def ffn_block(c, nxt, first, last_block):
                for j in range(HC):
                    if first and j == HC - 1:
                        for r in (2, 3):
                            rows_out(TURNS_ALL + r, r, four_x[:, nxt])
                    relu(c, j, first)
                    if first and j + 4 < HC:
                        take_signs(j + 4)
                    if not first and j == 1:
                        accumulator_out(c - 1, 1)
                        accumulator_out(c - 1, 3)
                    if first and j == HC - 2:
                        for r in (0, 1):
                            rows_out(TURNS_ALL + r, r, four_x[:, nxt])
                    if not first and not last_block and 8 <= j < 12:
                        rows_out(TURNS_ALL + RT * c + j - 8, j - 8, four_x[:, nxt])

            ffn_block(0, 1, True, False)
            with act.Fori(1, BATCH - 1) as c:
                ffn_block(c, c + 1, False, False)
            ffn_block(BATCH - 1, 0, False, True)
            act.wait_ge(down_done, last_down(LAST_POOL))
            act.activation(scaled[:, LAST_POOL, :], wide(LAST_POOL), ACT.Copy).then_inc(acc_out, 1)

        @block.vector
        def _(dve):
            def four(bank):
                return bank.rearrange("p (k n) -> p k n", n=P)

            def turn_out(n, bank, dst):
                dve.wait_ge(turn_hi, n + 1)
                dve.tensor_tensor(dst(LO), four(bank), dst(HI).bitcast(F32), ALU.subtract).then_inc(turn_lo, 1)

            def proj_out(n, k, dst, scale=None):
                dve.wait_ge(proj_hi, n + 1)
                if scale is None:
                    dve.tensor_tensor(dst(LO), proj[:, k, :], dst(HI).bitcast(F32), ALU.subtract
                                      ).then_inc(proj_lo, 1)
                else:
                    dve.scalar_tensor_tensor(dst(LO), proj[:, k, :], scale, dst(HI).bitcast(F32),
                                             ALU.mult, ALU.subtract).then_inc(proj_lo, 1)

            def chunk(buf, c):
                return lambda s: buf[:, s, c, :]

            def part(buf, r):
                return lambda s: buf[:, s, :, r * P:(r + 1) * P]

            def maxima(b, t):
                dve.wait_ge(scored, RT * b + t + 1)
                dve.reduce_max(neg_max[:, t:t + 1], score[t % 2][:, :, :].rearrange("p a n -> p (a n)"),
                               AX.X, negate=True).then_inc(max_done, 1)

            def probs_out(b, t):
                for half in range(2):
                    turn_out(turn0(b) + 2 * t + half, turn[:, half, :],
                             lambda s, half=half: probsT[:, s, 4 * half:4 * half + 4, t * P:(t + 1) * P])

            def norm_stats(n, tile0):
                for r in range(RT):
                    dve.bn_stats(stats[:, r, :], rows[:, tile0 + r, :]).then_inc(stats_done, 1)

            def norm_moments(n):
                for r in range(RT):
                    dve.bn_aggr(mean_var[:, r, :], stats[:, r, :]).then_inc(meanvar_done, 1)

            def norm_rows(n, tile0):
                dve.wait_ge(rstd_done, n + 1)
                for r in range(RT):
                    dve.tensor_scalar(normed[:, r, :], rows[:, tile0 + r, :], mean_var[:, r, 0:1], rstd[:, r:r + 1],
                                      ALU.subtract, ALU.mult).then_inc(normed_done, 1)

            def take_signs(j):
                dve.wait_ge(signs_turned, j + 1)
                dve.tensor_copy(signs[:, j].rearrange("p k n -> p (k n)"), turn[:, j % 2, :].bitcast(BF16)
                                ).then_inc(signs_ready, 1)

            def batch(b, next_tile0, last_batch):
                n, m = turn0(b), proj0(b)
                maxima(b, 0)
                maxima(b, 1)
                probs_out(b, 0)
                if not last_batch:
                    dve.wait_ge(xrest_in, 16 * (BATCH - 1))
                norm_stats(b + 1, next_tile0)
                dve.wait_ge(stats_done, RT * (b + 1) + RT)
                maxima(b, 2)
                norm_moments(b + 1)
                probs_out(b, 1)
                maxima(b, 3)
                probs_out(b, 2)
                norm_rows(b + 1, next_tile0)
                proj_out(m, 0, chunk(new_side, 0))
                proj_out(m + 1, 1, chunk(new_side, 1))
                probs_out(b, 3)
                proj_out(m + 2, 0, chunk(new_side, 2))
                proj_out(m + 3, 1, chunk(new_side, 3))
                dve.wait_ge(exp_done, RT * b + RT)
                dve.reciprocal(row_inv[:, :], row_sum[:, :]).then_inc(inv_done, 1)
                dve.wait_ge(inv_done, b + 1)
                dve.tensor_scalar(row_gain[:, :], row_inv[:, :], gates[:, 0:1], None, ALU.mult
                                  ).then_inc(rowgain_done, 1)
                for e in range(DC):
                    proj_out(m + 4 + e, e % 2, chunk(qT, e))
                    if e in (1, 2):
                        for r in (2 * e - 2, 2 * e - 1):
                            turn_out(n + 2 * RT + r, turn[:, r % 2, :], part(xT, r))
                if not last_batch:
                    for r in range(RT):
                        turn_out(n + 3 * RT + r, turn[:, r % 2, :], part(ctx_side, r))
                else:
                    take_signs(0)
                    take_signs(1)
                dve.wait_ge(rowgain_done, b + 1)
                for r in range(RT):
                    dve.wait_ge(wo_done, RT * b + r + 1)
                    mine = rows[:, RT * b + r, :]
                    dve.scalar_tensor_tensor(mine, wide(r), row_gain[:, r:r + 1], mine, ALU.mult, ALU.add
                                             ).then_inc(attended, 1)
                if last_batch:
                    return
                for e in range(DC):
                    proj_out(m + 8 + e, e % 2, chunk(new_side, e))
                for e in range(DC):
                    proj_out(m + 12 + e, e % 2, chunk(qT, e), SCALE)

            for r in range(RT):
                dve.wait_ge(x0_in[r], 16)
                dve.bn_stats(stats[:, r, :], rows[:, r, :]).then_inc(stats_done, 1)
            dve.wait_ge(stats_done, RT)
            norm_moments(0)
            norm_rows(0, 0)
            for r in range(RT):
                turn_out(T_WK + r, first_turn_bank(T_WK + r), part(weights[:, W_K], r))
            for r in range(RT):
                turn_out(T_X0 + r, first_turn_bank(T_X0 + r), part(xT, r))
            for m in range(2 * DC):
                if m < DC:
                    proj_out(m, m % 2, chunk(new_side, m))
                else:
                    proj_out(m, m % 2, chunk(qT, m - DC), SCALE)
                for n in turns_after(m):
                    dst = weights[:, n // RT - 2] if n >= T_WV else weights[:, W_Q] if n < T_C0 else ctx_side
                    turn_out(n, first_turn_bank(n), part(dst, n % RT))
            dve.wait_ge(tanh_done, 1)
            dve.tensor_tensor(ffn_gain[:, :], gates[:, 1:2], gates_raw[:, 2:3], ALU.mult).then_inc(gain_done, 1)
            dve.wait_ge(gain_done, 1)
            dve.tensor_scalar(out_gain[:, :], out_gain[:, :], ffn_gain[:, 0:1], None, ALU.mult
                              ).then_inc(gain_done, 1)

            with dve.Fori(0, BATCH - 1) as b:
                batch(b, RT * b + RT, False)
            batch(BATCH - 1, 0, True)

            def split_hidden(c, j, first):
                g = HC * c + j
                slot = hid_split[:, j % HR]
                dve.wait_ge(relu_done, g + 1)
                if not (first and j < HR):
                    dve.wait_ge(down_done, RT * (g - HR + 1))
                dve.tensor_copy(slot[:, HI, :], hid[:, j % HR, :]).then_inc(hid_hi, 1)
                dve.wait_ge(hid_hi, g + 1)
                dve.tensor_tensor(slot[:, LO, :], hid[:, j % HR, :], slot[:, HI, :].bitcast(F32), ALU.subtract
                                  ).then_inc(hid_ready, 1)

            def scale_even(c, r):
                dve.wait_ge(down_done, RT * (HC * c + HC - 1) + r + 1)
                dve.tensor_tensor(scaled[:, r, :], wide(r), out_gain[:, :], ALU.mult).then_inc(acc_scaled, 1)

            def scale_odd(c, r):
                dve.wait_ge(acc_out, 2 * c + r // 2 + 1)
                dve.tensor_tensor(scaled[:, r, :], scaled[:, r, :], out_gain[:, :], ALU.mult).then_inc(odd_scaled, 1)

            def add_rows(c, r, scaled_sem):
                dve.wait_ge(scaled_sem, 2 * c + r // 2 + 1)
                mine = rows[:, RT * c + r, :]
                dve.tensor_tensor(mine, mine, scaled[:, r, :], ALU.add).then_inc(out_ready, 1)

            def ffn_block(c, nxt, first, last_block):
                for j in range(HC):
                    if first and j + 2 < HC:
                        take_signs(j + 2)
                    if not last_block and j == 5:
                        dve.wait_ge(stats_done, RT * (BATCH + c + 2))
                    if first and j == HC - 1:
                        for r in (2, 3):
                            turn_out(TURNS_ALL + r, turn[:, r % 2, :], part(four_x[:, nxt], r))
                    split_hidden(c, j, first)
                    if not last_block and j == 5:
                        norm_moments(BATCH + c + 1)
                    if not first and j == 1:
                        scale_even(c - 1, 0)
                        scale_even(c - 1, 2)
                    if not first and j == 2:
                        add_rows(c - 1, 0, acc_scaled)
                        scale_odd(c - 1, 1)
                        add_rows(c - 1, 1, odd_scaled)
                    if not first and j == 3:
                        add_rows(c - 1, 2, acc_scaled)
                        scale_odd(c - 1, 3)
                        add_rows(c - 1, 3, odd_scaled)
                    if not last_block and j == 4:
                        norm_stats(BATCH + c + 1, RT * c + RT)
                    if not last_block and j == 6:
                        norm_rows(BATCH + c + 1, RT * c + RT)
                    if first and j == HC - 2:
                        for r in (0, 1):
                            turn_out(TURNS_ALL + r, turn[:, r % 2, :], part(four_x[:, nxt], r))
                    if not first and not last_block and 8 <= j < 12:
                        turn_out(TURNS_ALL + RT * c + j - 8, turn[:, (j - 8) % 2, :], part(four_x[:, nxt], j - 8))

            ffn_block(0, 1, True, False)
            with dve.Fori(1, BATCH - 1) as c:
                ffn_block(c, c + 1, False, False)
            ffn_block(BATCH - 1, 0, False, True)
            for r in LAST_DVE:
                dve.wait_ge(down_done, last_down(r))
                dve.tensor_tensor(scaled[:, r, :], wide(r), out_gain[:, :], ALU.mult).then_inc(last_scaled, 1)
                dve.wait_ge(last_scaled, LAST_DVE.index(r) + 1)
                mine = rows[:, LAST + r, :]
                dve.tensor_tensor(mine, mine, scaled[:, r, :], ALU.add).then_inc(out_ready, 1)


_INS = ['x', 'ctx_2048', 'g_xattn', 'g_ffn', 'L0_xattn_wq', 'L0_xattn_wk', 'L0_xattn_wv', 'L0_xattn_wo',
        'L0_ffn_up_weight', 'L0_ffn_down_weight', 'L0_ffn_up_scale', 'L0_ffn_down_scale', 'L0_ffn_output_scale']


def kernel(**inputs):
    import numpy as _np
    import concourse.bacc as _bacc
    from concourse import mybir as _mybir
    from concourse.bass_utils import run_bass_kernel_spmd as _run

    nc = _bacc.Bacc("TRN2", target_bir_lowering=False, num_devices=1, dynamic_dma_scratch_size=256)
    arrays, args = {}, []
    for name in _INS:
        a = _np.ascontiguousarray(inputs[name])
        arrays[f"in_{name}"] = a
        args.append(nc.dram_tensor(f"in_{name}", a.shape, _mybir.dt.from_np(a.dtype), kind="ExternalInput").ap())
    shape = inputs['x'].shape
    args.append(nc.dram_tensor("result", tuple(shape), _mybir.dt.float32, kind="ExternalOutput").ap())
    gated_block(nc, *args)
    r = _run(nc, [arrays], core_ids=[0])
    return r.results[0]["result"]
```
